# Optimizing a Trainium2 kernel written in Bass

```python
import numpy as np
import jax
import jax.numpy as jnp

def _softmax(x, axis=-1):
    return jax.nn.softmax(x, axis=axis)

def _gelu(x):
    return jax.nn.gelu(x, approximate=True)

def _silu(x):
    return jax.nn.silu(x)

def _sigmoid(x):
    return jax.nn.sigmoid(x)

def _layernorm(x, axis=-1, eps=1e-05):
    m = jnp.mean(x, axis=axis, keepdims=True)
    v = jnp.var(x, axis=axis, keepdims=True)
    return (x - m) / jnp.sqrt(v + eps)

def _scatter_add(tgt, idx, src, axis=0):
    return tgt.at[idx].add(src)

def _segment_sum(src, seg, n):
    return jax.ops.segment_sum(src, seg, n)
kernel_name = 'mk_prb_d1_jaxref_r4_5ae8c5'

def setup_inputs(seed: int=0):
    np.random.seed(seed)
    _w = jnp.asarray

    def _L0_attn_setup():
        import jax, jax.numpy as jnp
        import numpy as np
        DIM = 512
        NUM_HEADS = 16
        HEAD_DIM = 128
        T_LEN = 512
        W_MAX = 1.0

        def _init_linear(key, out_f, in_f):
            std = 0.5 * in_f ** (-0.5)
            bound = 3.0 ** 0.5 * std
            return jax.random.uniform(key, (out_f, in_f), jnp.float32, -bound, bound)

        def _rope_tables(T, dh, dtype):
            af = (1.0 / 1024.0) ** jnp.linspace(0.0, 1.0, dh // 4, dtype=jnp.float32)
            af = jnp.concatenate([af, jnp.zeros(dh // 4, jnp.float32)])
            theta = jnp.arange(T, dtype=jnp.float32)[:, None] * af[None, :]
            return (jnp.cos(theta), jnp.sin(theta))

        def _apply_rope(x_BTHD, cos, sin):
            x = x_BTHD.astype(jnp.float32)
            x1, x2 = jnp.split(x, 2, axis=-1)
            c = cos[None, :, None, :]
            s = sin[None, :, None, :]
            y1 = x1 * c + x2 * s
            y2 = -x1 * s + x2 * c
            return jnp.concatenate([y1, y2], axis=-1).astype(x_BTHD.dtype)
        key = jax.random.key(seed)
        kx, kq, kk, kv, ko = jax.random.split(key, 5)
        hdim = NUM_HEADS * HEAD_DIM
        return {'x': jax.random.normal(kx, (1, T_LEN, DIM), jnp.float32), 'Wq': _init_linear(kq, hdim, DIM), 'Wk': _init_linear(kk, hdim, DIM), 'Wv': _init_linear(kv, hdim, DIM), 'Wo': _init_linear(ko, DIM, hdim)}
    _L0_attn_in = _L0_attn_setup()

    def _L0_ffn_setup():
        import jax, jax.numpy as jnp
        import numpy as np
        HIDDEN = 512
        INTER = 1408
        B, S = (2, 512)

        def _ternary(key, shape):
            return jax.random.randint(key, shape, -1, 2).astype(jnp.float32)
        key = jax.random.key(seed)
        ks = jax.random.split(key, 7)
        x = jax.random.normal(ks[0], (B, S, HIDDEN), dtype=jnp.float32)
        gate_w = _ternary(ks[1], (INTER, HIDDEN))
        up_w = _ternary(ks[2], (INTER, HIDDEN))
        down_w = _ternary(ks[3], (HIDDEN, INTER))
        gate_s = jax.random.uniform(ks[4], (INTER,), minval=0.01, maxval=0.1, dtype=jnp.float32)
        up_s = jax.random.uniform(ks[5], (INTER,), minval=0.01, maxval=0.1, dtype=jnp.float32)
        down_s = jax.random.uniform(ks[6], (HIDDEN,), minval=0.01, maxval=0.1, dtype=jnp.float32)
        return {'x': x, 'gate_w': gate_w, 'up_w': up_w, 'down_w': down_w, 'gate_s': gate_s, 'up_s': up_s, 'down_s': down_s}
    _L0_ffn_in = _L0_ffn_setup()
    _d = {'L0_attn_x': _L0_attn_in['x'], 'L0_attn_Wq': _L0_attn_in['Wq'], 'L0_attn_Wk': _L0_attn_in['Wk'], 'L0_attn_Wv': _L0_attn_in['Wv'], 'L0_attn_Wo': _L0_attn_in['Wo'], 'L0_ffn_gate_w': _L0_ffn_in['gate_w'], 'L0_ffn_up_w': _L0_ffn_in['up_w'], 'L0_ffn_down_w': _L0_ffn_in['down_w'], 'L0_ffn_gate_s': _L0_ffn_in['gate_s'], 'L0_ffn_up_s': _L0_ffn_in['up_s'], 'L0_ffn_down_s': _L0_ffn_in['down_s']}
    _x0 = _d['L0_attn_x']
    _d['L0_attn_x'] = jax.random.normal(jax.random.fold_in(jax.random.key(seed), 1), (8, 512, 512), dtype=_x0.dtype)
    del _x0
    return _d

def reference(L0_attn_x, L0_attn_Wq, L0_attn_Wk, L0_attn_Wv, L0_attn_Wo, L0_ffn_gate_w, L0_ffn_up_w, L0_ffn_down_w, L0_ffn_gate_s, L0_ffn_up_s, L0_ffn_down_s):

    def _L0_attn_ref(x, Wq, Wk, Wv, Wo):
        import jax, jax.numpy as jnp
        import numpy as np
        DIM = 512
        NUM_HEADS = 16
        HEAD_DIM = 128
        T_LEN = 512
        W_MAX = 1.0

        def _init_linear(key, out_f, in_f):
            std = 0.5 * in_f ** (-0.5)
            bound = 3.0 ** 0.5 * std
            return jax.random.uniform(key, (out_f, in_f), jnp.float32, -bound, bound)

        def _rope_tables(T, dh, dtype):
            af = (1.0 / 1024.0) ** jnp.linspace(0.0, 1.0, dh // 4, dtype=jnp.float32)
            af = jnp.concatenate([af, jnp.zeros(dh // 4, jnp.float32)])
            theta = jnp.arange(T, dtype=jnp.float32)[:, None] * af[None, :]
            return (jnp.cos(theta), jnp.sin(theta))

        def _apply_rope(x_BTHD, cos, sin):
            x = x_BTHD.astype(jnp.float32)
            x1, x2 = jnp.split(x, 2, axis=-1)
            c = cos[None, :, None, :]
            s = sin[None, :, None, :]
            y1 = x1 * c + x2 * s
            y2 = -x1 * s + x2 * c
            return jnp.concatenate([y1, y2], axis=-1).astype(x_BTHD.dtype)
        B, T, _ = x.shape
        H, Dh = (NUM_HEADS, HEAD_DIM)
        scale = Dh ** 0.5 / W_MAX ** 2 / Dh
        q = (x @ Wq.T).reshape(B, T, H, Dh)
        k = (x @ Wk.T).reshape(B, T, H, Dh)
        v = (x @ Wv.T).reshape(B, T, H, Dh)
        cos, sin = _rope_tables(T, Dh, x.dtype)
        q = _apply_rope(q, cos, sin)
        k = _apply_rope(k, cos, sin)
        scores = jnp.einsum('bthd,bshd->bhts', q, k) * scale
        causal = jnp.tril(jnp.ones((T, T), bool))
        scores = jnp.where(causal[None, None], scores, -jnp.inf)
        attn = jax.nn.softmax(scores, axis=-1)
        y = jnp.einsum('bhts,bshd->bthd', attn, v).reshape(B, T, H * Dh)
        return y / 3.0 @ Wo.T

    def _L0_ffn_ref(x, gate_w, up_w, down_w, gate_s, up_s, down_s):
        import jax, jax.numpy as jnp
        import numpy as np
        HIDDEN = 512
        INTER = 1408
        B, S = (2, 512)

        def _ternary(key, shape):
            return jax.random.randint(key, shape, -1, 2).astype(jnp.float32)
        b, s, h = x.shape
        xf = x.reshape(b * s, h)
        g = jnp.einsum('th,ih->ti', xf, gate_w) * gate_s
        u = jnp.einsum('th,ih->ti', xf, up_w) * up_s
        hdn = jax.nn.silu(g) * u
        out = jnp.einsum('ti,hi->th', hdn, down_w) * down_s
        return out.reshape(b, s, -1)
    x = L0_attn_x
    xn = _layernorm(x, axis=-1)
    x = x + _L0_attn_ref(xn, L0_attn_Wq, L0_attn_Wk, L0_attn_Wv, L0_attn_Wo) + _L0_ffn_ref(xn, L0_ffn_gate_w, L0_ffn_up_w, L0_ffn_down_w, L0_ffn_gate_s, L0_ffn_up_s, L0_ffn_down_s)
    return x

_drawn_inputs = setup_inputs


def setup_inputs(seed=0):
    import zlib

    import numpy as np

    out = dict(_drawn_inputs(seed))
    spreads = {}
    factors = {'L0_attn_Wq': 8.0, 'L0_attn_Wk': 8.0, 'L0_attn_Wv': 8.0, 'L0_attn_Wo': 8.0}
    for name, (base, spread) in spreads.items():
        noise = np.random.default_rng([zlib.crc32(name.encode()), seed]).standard_normal(out[name].shape)
        drawn = base * np.exp(spread * noise) if base else spread * noise
        out[name] = jnp.asarray(drawn.astype(out[name].dtype))
    for name, factor in factors.items():
        out[name] = (out[name] * factor).astype(out[name].dtype)
    return out
```

```python
from contextlib import ExitStack

import concourse.bass as bass
from concourse import mybir

ALU = mybir.AluOpType
ACT = mybir.ActivationFunctionType
F32 = mybir.dt.float32
F32R = mybir.dt.float32r

P = 128
B = 8
T = 512
D = 512
H = 16
DH = 128
INTER = 1408
TT = T // P
KD = D // P
J = INTER // P
HG = 4
G = H // HG
ROT = DH // 4
EPS = 1e-5
SCALE = float(DH) ** 0.5 / DH
HI, LO = 0, 1
NEXT = 5

SCORE_AT = {3: (0, 0, 512), 2: (1, 0, 384), 0: (1, 384, 128), 1: (2, 0, 256)}
SCORE_ORDER = [[3], [2, 0], [1]]
PROB_AT = {j: SCORE_AT[TT - 1 - j] for j in range(TT)}
BANK_WIDTH = [512, 512, 256]
BANK_START = [0, 512, 1024]
CAUSAL = sum(BANK_WIDTH)

C_MASK, C_IDENT, C_COS, C_SIN = 0, T, T + P, 2 * T + P


def wait_alone(eng, sem, count, passed):
    eng.wait_ge(sem, count)
    eng.sem_inc(passed, 1)


def products(pe, out, w, x, start, stop):
    pe.matmul(out, w(HI), x(LO), start=start, stop=False)
    pe.matmul(out, w(LO), x(HI), start=False, stop=False)
    return pe.matmul(out, w(HI), x(HI), start=False, stop=stop)


def ffn_phase(nc, x_dram, ffnw_dram, ffns_dram, down_dram, const_dram, xt_dram, out):
    with ExitStack() as ctx:
        def sb(name, shape, dt=F32):
            return ctx.enter_context(nc.sbuf_tensor(name, shape, dt))

        def ps(name, shape):
            return ctx.enter_context(nc.psum_tensor(name, shape, F32))

        def sem(name):
            return ctx.enter_context(nc.semaphore(name))

        w = sb("ffn_w", [P, 2, J, 3, 512], F32R)
        w_stage = sb("ffn_w_stage", [P, 3, 512])
        xt = sb("ffn_xt", [P, 2, 2, KD, T], F32R)
        xin = sb("ffn_xin", [P, 2, TT, D])
        xn = sb("ffn_xn", [P, 2, D])
        hid = sb("ffn_hid", [P, 2, 2, T], F32R)
        silu = sb("ffn_silu", [P, T])
        down_s = sb("ffn_down_s", [P, D])
        ident = sb("ffn_ident", [P, P])
        gu_s = sb("ffn_gu_s", [P, 2, J])
        stats = sb("ffn_stats", [P, TT, 6])
        mv = sb("ffn_mv", [P, TT, 2])
        veps = sb("ffn_veps", [P, TT])
        rstd = sb("ffn_rstd", [P, TT])
        half = sb("ffn_half", [P, TT])

        p_gate = ps("p_gate", [P, T])
        p_up = ps("p_up", [P, T])
        p_tr = [ps(f"p_tr{i}", [P, KD, P]) for i in range(2)]
        p_down = [ps(f"p_down{t}", [P, D]) for t in range(TT)]

        const_in = sem("f_const_in")
        down_s_in = sem("f_down_s_in")
        half_set = sem("f_half_set")
        x_in = [sem(f"f_x_in{i}") for i in range(2)]
        w_in = [sem(f"f_w_in{i}") for i in range(3)]
        w_hi = sem("f_w_hi")
        w_lo = sem("f_w_lo")
        st = sem("f_stats")
        passed = sem("f_passed")
        ag = sem("f_aggr")
        ve = sem("f_veps")
        rs = sem("f_rstd")
        xn_done = sem("f_xn")
        tr_done = sem("f_tr")
        tr_hi = sem("f_tr_hi")
        tr_lo = sem("f_tr_lo")
        gate_done = sem("f_gate")
        up_done = sem("f_up")
        silu_done = sem("f_silu")
        hid_done = sem("f_hid")
        hid_hi = sem("f_hid_hi")
        hid_lo = sem("f_hid_lo")
        down_done = sem("f_down")
        scaled = sem("f_scaled")
        sum_done = sem("f_sum")
        xt_out = sem("f_xt_out")
        sum_out = sem("f_sum_out")
        block = ctx.enter_context(nc.Block())

        @block.sync
        def _(sp):
            sp.dma_start(xin[:, 0], x_dram[0]).then_inc(x_in[0], 16)
            sp.dma_start(ident[:], const_dram[:, C_IDENT:C_IDENT + P]).then_inc(const_in, 16)
            sp.dma_start(gu_s[:], ffns_dram).then_inc(const_in, 16)
            for u in range(3 * J):
                if u >= 3:
                    sp.wait_ge(w_lo, u - 2)
                sp.dma_start(w_stage[:, u % 3], ffnw_dram[u]).then_inc(w_in[u % 3], 16)
                if u == 3:
                    sp.dma_start(down_s[:], down_dram).then_inc(down_s_in, 16)
                    sp.dma_start(xin[:, 1], x_dram[1]).then_inc(x_in[1], 16)

            def row(b, q):
                sp.wait_ge(xt_out, 16 * b)
                sp.wait_ge(tr_lo, TT * b + TT)
                sp.dma_start(xt_dram[b], xt[:, q].bitcast(F32)).then_inc(xt_out, 16)
                sp.wait_ge(sum_done, TT * b + TT)
                sp.dma_start(out[b], xin[:, q]).then_inc(sum_out, 16)

            def load(b, q):
                sp.wait_ge(sum_out, 16 * b - 16)
                sp.dma_start(xin[:, q], x_dram[b]).then_inc(x_in[q], 16)

            row(0, 0)
            with sp.Fori(0, (B - 2) // 2) as i:
                load(2 * i + 2, 0)
                row(2 * i + 1, 1)
                load(2 * i + 3, 1)
                row(2 * i + 2, 0)
            row(B - 1, 1)
            sp.wait_ge(xt_out, 16 * B)
            sp.wait_ge(sum_out, 16 * B)

        @block.tensor
        def _(pe):
            def transposes(b, q, t):
                pe.wait_ge(xn_done, TT * b + t + 1)
                if t >= 2:
                    pe.wait_ge(tr_lo, TT * b + t - 1)
                for k in range(KD):
                    mm = pe.transpose(p_tr[t % 2][:, k], xn[:, t % 2, k * P:(k + 1) * P], ident[:])
                mm.then_inc(tr_done, 1)

            def gate_up(b, q, j):
                pe.wait_ge(w_lo, 3 * j + 2)
                if j == 0:
                    pe.wait_ge(tr_lo, TT * b + TT)
                for out_, c, ready, done in ((p_gate, 0, silu_done, gate_done), (p_up, 1, hid_lo, up_done)):
                    pe.wait_ge(ready, J * b + j)
                    for k in range(KD):
                        mm = products(pe, out_[:], lambda h: w[:, h, j, c, k * P:(k + 1) * P],
                                      lambda h: xt[:, q, h, k], k == 0, k == KD - 1)
                    mm.then_inc(done, 1)

            def down(b, q, j):
                pe.wait_ge(w_lo, 3 * j + 3)
                pe.wait_ge(hid_lo, J * b + j + 1)
                if j == 0:
                    pe.wait_ge(sum_done, TT * b)
                r = (q + j) % 2
                for t in range(TT):
                    mm = products(pe, p_down[t][:], lambda h: hid[:, r, h, t * P:(t + 1) * P],
                                  lambda h: w[:, h, j, 2], j == 0, j == J - 1)
                mm.then_inc(down_done, 1)

            def row(b, q, first=False, last=False):
                for j in range(J):
                    gate_up(b, q, j)
                    if j:
                        down(b, q, j - 1)
                    elif not first:
                        down(b - 1, 1 - q, J - 1)
                    if NEXT <= j < NEXT + TT and not last:
                        transposes(b + 1, 1 - q, j - NEXT)

            pe.wait_ge(const_in, 32)
            for t in range(TT):
                transposes(0, 0, t)
            row(0, 0, first=True)
            with pe.Fori(0, (B - 2) // 2) as i:
                row(2 * i + 1, 1)
                row(2 * i + 2, 0)
            row(B - 1, 1, last=True)
            down(B - 1, 1, J - 1)

        @block.scalar
        def _(act):
            def split_w(u):
                act.wait_ge(w_in[u % 3], 16 * (u // 3) + 16)
                nc.scalar.activation(w[:, HI, u // 3, u % 3], w_stage[:, u % 3], ACT.Copy).then_inc(w_hi, 1)

            def split_x(b, q, t):
                act.wait_ge(tr_done, TT * b + t + 1)
                nc.scalar.activation(xt[:, q, HI, :, t * P:(t + 1) * P], p_tr[t % 2][:],
                                     ACT.Copy).then_inc(tr_hi, 1)

            def hidden(b, q, j):
                act.wait_ge(gate_done, J * b + j + 1)
                act.wait_ge(hid_done, J * b + j)
                nc.scalar.activation(silu[:], p_gate[:], ACT.Silu,
                                     scale=gu_s[:, 0, j:j + 1]).then_inc(silu_done, 1)
                act.wait_ge(hid_done, J * b + j + 1)
                nc.scalar.activation(hid[:, (q + j) % 2, HI], p_up[:], ACT.Copy).then_inc(hid_hi, 1)

            def row(b, q, first=False, last=False):
                for j in range(J):
                    if first and j < J - 1:
                        for c in range(3):
                            split_w(3 * j + 3 + c)
                    hidden(b, q, j)
                    if j == NEXT and not last:
                        act.wait_ge(xt_out, 16 * b)
                    if NEXT <= j < NEXT + TT and not last:
                        split_x(b + 1, 1 - q, j - NEXT)

            act.wait_ge(const_in, 32)
            split_w(0)
            split_w(1)
            split_w(2)
            for t in range(TT):
                split_x(0, 0, t)
            row(0, 0, first=True)
            with act.Fori(0, (B - 2) // 2) as i:
                row(2 * i + 1, 1)
                row(2 * i + 2, 0)
            row(B - 1, 1, last=True)

        @block.gpsimd
        def _(pool):
            nc.gpsimd.memset(half[:], -0.5).then_inc(half_set, 1)
            pool.wait_ge(half_set, 1)

            def split_w(u):
                pool.wait_ge(w_hi, u + 1)
                nc.gpsimd.tensor_tensor(w[:, LO, u // 3, u % 3], w_stage[:, u % 3],
                                        w[:, HI, u // 3, u % 3].bitcast(F32), ALU.subtract).then_inc(w_lo, 1)

            def root(b):
                pool.wait_ge(ve, b + 1)
                nc.gpsimd.tensor_tensor(rstd[:], veps[:], half[:], ALU.pow).then_inc(rs, 1)

            root(0)
            for u in range(3 * NEXT + 3):
                split_w(u)
            root(1)
            for u in range(3 * NEXT + 3, 3 * J):
                split_w(u)
            with pool.Fori(2, B) as b:
                root(b)

        @block.vector
        def _(dve):
            def statistics(b, q):
                dve.wait_ge(x_in[q], 8 * b + 16 - 8 * q)
                for t in range(TT):
                    ins = nc.vector.bn_stats(stats[:, t], xin[:, q, t])
                ins.then_inc(st, 1)
                wait_alone(dve, st, b + 1, passed)
                for t in range(TT):
                    ins = nc.vector.bn_aggr(mv[:, t], stats[:, t])
                ins.then_inc(ag, 1)
                dve.wait_ge(ag, b + 1)
                nc.vector.tensor_scalar(veps[:], mv[:, :, 1], EPS, None, ALU.add).then_inc(ve, 1)

            def normalise(b, q, t):
                dve.wait_ge(rs, b + 1)
                if t >= 2:
                    dve.wait_ge(tr_done, TT * b + t - 1)
                nc.vector.tensor_scalar(xn[:, t % 2], xin[:, q, t], mv[:, t, 0:1], rstd[:, t:t + 1],
                                        ALU.subtract, ALU.mult).then_inc(xn_done, 1)

            def split_x(b, q, t):
                dve.wait_ge(tr_hi, TT * b + t + 1)
                s = slice(t * P, (t + 1) * P)
                nc.vector.tensor_tensor(xt[:, q, LO, :, s], p_tr[t % 2][:], xt[:, q, HI, :, s].bitcast(F32),
                                        ALU.subtract).then_inc(tr_lo, 1)

            def hidden(b, q, j):
                dve.wait_ge(silu_done, J * b + j + 1)
                dve.wait_ge(up_done, J * b + j + 1)
                nc.vector.scalar_tensor_tensor(p_up[:], p_up[:], gu_s[:, 1, j:j + 1], silu[:],
                                               ALU.mult, ALU.mult).then_inc(hid_done, 1)
                dve.wait_ge(hid_hi, J * b + j + 1)
                r = (q + j) % 2
                nc.vector.tensor_tensor(hid[:, r, LO], p_up[:], hid[:, r, HI].bitcast(F32),
                                        ALU.subtract).then_inc(hid_lo, 1)

            def sums(b, q):
                dve.wait_ge(down_done, J * b + J)
                for t in range(TT):
                    nc.vector.tensor_tensor(p_down[t][:], p_down[t][:], down_s[:], ALU.mult).then_inc(scaled, 1)
                for t in range(TT):
                    dve.wait_ge(scaled, TT * b + t + 1)
                    nc.vector.tensor_tensor(xin[:, q, t], p_down[t][:], xin[:, q, t],
                                            ALU.add).then_inc(sum_done, 1)

            def row(b, q, first=False, last=False):
                for j in range(J):
                    hidden(b, q, j)
                    if j == 0 and not first:
                        sums(b - 1, 1 - q)
                    if last:
                        continue
                    if j == NEXT - 1:
                        statistics(b + 1, 1 - q)
                        normalise(b + 1, 1 - q, 0)
                        normalise(b + 1, 1 - q, 1)
                    if NEXT <= j < NEXT + TT:
                        split_x(b + 1, 1 - q, j - NEXT)
                        if j - NEXT + 2 < TT:
                            normalise(b + 1, 1 - q, j - NEXT + 2)

            statistics(0, 0)
            normalise(0, 0, 0)
            normalise(0, 0, 1)
            for t in range(TT):
                split_x(0, 0, t)
                if t < 2:
                    normalise(0, 0, t + 2)
            dve.wait_ge(const_in, 32)
            dve.wait_ge(down_s_in, 16)
            row(0, 0, first=True)
            with dve.Fori(0, (B - 2) // 2) as i:
                row(2 * i + 1, 1)
                row(2 * i + 2, 0)
            row(B - 1, 1, last=True)
            sums(B - 1, 1)


def attention_phase(nc, wqk_dram, wv_dram, wo_dram, const_dram, xt_dram, out):
    with ExitStack() as ctx:
        def sb(name, shape, dt=F32):
            return ctx.enter_context(nc.sbuf_tensor(name, shape, dt))

        def ps(name, shape):
            return ctx.enter_context(nc.psum_tensor(name, shape, F32))

        def sem(name):
            return ctx.enter_context(nc.semaphore(name))

        w_qk = sb("w_qk", [P, 2, HG, 2, KD, DH], F32R)
        w_v = sb("w_v", [P, 2, KD, HG * DH], F32R)
        w_o = sb("w_o", [P, 2, HG, D], F32R)
        w_stage = sb("w_stage", [P, 2, 512])
        xt = sb("xt", [P, 2, 2, KD, T], F32R)
        v = sb("v", [P, 2, 2, TT, HG * DH], F32R)
        y = sb("y", [P, 2, 2, HG, T], F32R)
        qk = sb("qk", [P, 2, 2, T], F32R)
        probs = sb("probs", [P, CAUSAL])
        probs_t = sb("probs_t", [P, 2, CAUSAL], F32R)
        swap = sb("swap", [2 * ROT, 2, T])
        mask = sb("mask", [P, T])
        ident = sb("ident", [P, P])
        cos = sb("cos", [2 * ROT, T])
        sin = sb("sin", [2 * ROT, T])
        acc = sb("acc", [P, TT, D])
        neg_max = sb("neg_max", [P, TT])
        row_sum = sb("row_sum", [P, TT])
        inv_sum = sb("inv_sum", [P, TT])

        p_sc = [ps(f"p_sc{i}", [P, 512]) for i in range(3)]
        p_qk = [ps("p_q", [P, T]), ps("p_k", [P, T])]
        p_v = ps("p_v", [P, HG * DH])
        p_y = ps("p_y", [P, T])
        p_o = ps("p_o", [P, D])

        const_in = sem("const_in")
        x_in = [sem(f"x_in{i}") for i in range(2)]
        w_in = [sem(f"w_in{i}") for i in range(2)]
        w_hi = sem("w_hi")
        w_lo = sem("w_lo")
        qk_done = [sem("q_done"), sem("k_done")]
        qk_swap = [sem("q_swap"), sem("k_swap")]
        qk_sin = [sem("q_sin"), sem("k_sin")]
        qk_cos = [sem("q_cos"), sem("k_cos")]
        qk_rope = [sem("q_rope"), sem("k_rope")]
        qk_hi = [sem("q_hi"), sem("k_hi")]
        qk_lo = [sem("q_lo"), sem("k_lo")]
        v_done = sem("v_done")
        v_hi = sem("v_hi")
        v_lo = sem("v_lo")
        score_done = sem("score_done")
        dve_passed = sem("dve_passed")
        pool_passed = sem("pool_passed")
        max_done = sem("max_done")
        exp_done = sem("exp_done")
        inv_done = sem("inv_done")
        prob_done = sem("prob_done")
        pt_done = sem("pt_done")
        pt_hi = sem("pt_hi")
        pt_lo = sem("pt_lo")
        y_done = sem("y_done")
        y_hi = sem("y_hi")
        y_lo = sem("y_lo")
        o_done = sem("o_done")
        acc_in = [sem(f"acc_in{t}") for t in range(TT)]
        acc_done = sem("acc_done")
        acc_out = [sem(f"acc_out{t}") for t in range(TT)]
        block = ctx.enter_context(nc.Block())

        ONE = 1
        UNITS = 4 * HG
        LOAD_AT = {0: [0, 1, 2, 3], 1: [4, 5, 6, 7], 2: [8, 9], 3: [10, 11]}

        def w_part(u, part):
            if u < KD:
                return w_v[:, part, u]
            if u < KD + 2 * HG:
                return w_qk[:, part, (u - KD) // 2, (u - KD) % 2]
            return w_o[:, part, u - KD - 2 * HG]

        @block.sync
        def _(sp):
            def load_unit(g, u, first=False):
                gw = 0 if first else sp.snap(g % G)
                if not (first and u < 2):
                    sp.wait_ge(w_lo, g * UNITS + (u - 1))
                if u < KD:
                    src = wv_dram[gw, u]
                elif u < KD + 2 * HG:
                    src = wqk_dram[gw, u - KD]
                else:
                    src = wo_dram[gw, u - KD - 2 * HG]
                sp.dma_start(w_stage[:, u % 2], src).then_inc(w_in[u % 2], 16)

            def load_acc(b, n, t):
                sp.wait_ge(acc_out[t], 16 * n + ONE)
                sp.dma_start(acc[:, t], out[b, :, t]).then_inc(acc_in[t], 16)

            def store_acc(b, n, t):
                sp.wait_ge(acc_done, TT * n + t + 1 + ONE)
                sp.dma_start(out[b, :, t], acc[:, t]).then_inc(acc_out[t], 16)

            def load_x(b, n, q):
                sp.wait_ge(qk_done[1], HG * n - HG)
                sp.dma_start(xt[:, q].bitcast(F32), xt_dram[b]).then_inc(x_in[q], 16)

            def row(g, n, q, first=False, last=False, b=None):
                for h in range(HG):
                    if first:
                        load_unit(g, KD + 2 * HG + h)
                    if not first:
                        load_acc(b - 1, n - 1, h)
                        if h:
                            store_acc(b - 1, n - 1, h - 1)
                    if last:
                        for u in LOAD_AT[h]:
                            load_unit(g + 1, u)
                    if h == HG - 1:
                        load_x((b + 2) % B if isinstance(b, int) else b + 2, n + 2, q)
                if not first:
                    store_acc(b - 1, n - 1, HG - 1)

            for t in range(TT):
                sp.sem_inc(acc_out[t], ONE)
            sp.dma_start(xt[:, 0].bitcast(F32), xt_dram[0]).then_inc(x_in[0], 16)
            for u in range(KD + 2 * HG):
                load_unit(0, u, first=True)
                if u == KD:
                    for dst, at in ((mask, C_MASK), (ident, C_IDENT), (cos, C_COS), (sin, C_SIN)):
                        rows_, width = dst.shape
                        sp.dma_start(dst[:], const_dram[0:rows_, at:at + width]).then_inc(const_in, 16)
            sp.dma_start(xt[:, 1].bitcast(F32), xt_dram[1]).then_inc(x_in[1], 16)
            with sp.Fori(0, G) as g:
                row(g, g * B, 0, first=True, b=0)
                with sp.Fori(0, (B - 4) // 2) as i:
                    row(g, g * B + 2 * i + 1, 1, b=2 * i + 1)
                    row(g, g * B + 2 * i + 2, 0, b=2 * i + 2)
                row(g, g * B + (B - 3), 1, b=B - 3)
                row(g, g * B + (B - 2), 0, b=B - 2)
                row(g, g * B + (B - 1), 1, last=True, b=B - 1)
                for t in range(TT):
                    load_acc(B - 1, g * B + (B - 1), t)
                for t in range(TT):
                    store_acc(B - 1, g * B + (B - 1), t)
            for t in range(TT):
                sp.wait_ge(acc_out[t], 16 * G * B + ONE)
            for i in range(2):
                sp.wait_ge(x_in[i], 16 * (G * B // 2 + 1))

        ORDER = [i for tiles in SCORE_ORDER for i in tiles]

        def score_cols(i):
            bank, at, width = SCORE_AT[i]
            return slice(BANK_START[bank] + at, BANK_START[bank] + at + width)

        @block.tensor
        def _(pe):
            def project(g, n, q, h, c):
                pe.wait_ge(w_lo, UNITS * g + (KD + 2 * h + c + 1))
                pe.wait_ge(x_in[q], 8 * n + 16 - 8 * q)
                for k in range(KD):
                    mm = products(pe, p_qk[c][:], lambda a: w_qk[:, a, h, c, k],
                                  lambda a: xt[:, q, a, k], k == 0, k == KD - 1)
                mm.then_inc(qk_done[c], 1)

            def values(g, n, q, t):
                pe.wait_ge(w_lo, UNITS * g + KD)
                pe.wait_ge(x_in[q], 8 * n + 16 - 8 * q)
                pe.wait_ge(v_lo, TT * n + t + ONE)
                for k in range(KD):
                    mm = products(pe, p_v[:], lambda a: xt[:, q, a, k, t * P:(t + 1) * P],
                                  lambda a: w_v[:, a, k], k == 0, k == KD - 1)
                mm.then_inc(v_done, 1)

            def scores(s):
                pe.wait_ge(qk_lo[0], s + 1)
                pe.wait_ge(qk_lo[1], s + 1)
                for bank, tiles in enumerate(SCORE_ORDER):
                    for i in tiles:
                        _, at, width = SCORE_AT[i]
                        mm = products(pe, p_sc[bank][:, at:at + width],
                                      lambda a: qk[:, 0, a, i * P:(i + 1) * P],
                                      lambda a: qk[:, 1, a, 0:width], True, True)
                    mm.then_inc(score_done, 1)

            def transposes(s):
                pe.wait_ge(prob_done, TT * s + TT)
                for bank, tiles in enumerate(SCORE_ORDER):
                    for j in [TT - 1 - i for i in tiles]:
                        _, at, width = PROB_AT[j]
                        for i in range(j, TT):
                            block_at = score_cols(i).start + j * P
                            to = at + (i - j) * P
                            mm = pe.transpose(p_sc[bank][:, to:to + P], probs[:, block_at:block_at + P], ident[:])
                    mm.then_inc(pt_done, 1)

            def attend(n, q, h, s):
                pe.wait_ge(v_lo, TT * n + TT + ONE)
                pe.wait_ge(y_lo, s + ONE)
                for bank, tiles in enumerate(SCORE_ORDER):
                    pe.wait_ge(pt_lo, 3 * s + (bank + 1))
                    for j in [TT - 1 - i for i in tiles]:
                        _, at, width = PROB_AT[j]
                        cols = slice(BANK_START[bank] + at, BANK_START[bank] + at + width)
                        mm = products(pe, p_y[:, j * P:], lambda a: v[:, q, a, j, h * DH:(h + 1) * DH],
                                      lambda a: probs_t[:, a, cols], j == 0, j == TT - 1 - ORDER[-1])
                mm.then_inc(y_done, 1)

            def project_out(g, n, q, t):
                pe.wait_ge(w_lo, UNITS * g + UNITS)
                pe.wait_ge(y_lo, HG * n + HG + ONE)
                pe.wait_ge(acc_done, TT * n + t + ONE)
                for h in range(HG):
                    mm = products(pe, p_o[:], lambda a: y[:, q, a, h, t * P:(t + 1) * P],
                                  lambda a: w_o[:, a, h], h == 0, h == HG - 1)
                mm.then_inc(o_done, 1)

            def row(g, n, q, first=False, last=False):
                for h in range(HG):
                    s = HG * n + h
                    scores(s)
                    for c in range(2):
                        if h < HG - 1:
                            project(g, n, q, h + 1, c)
                        elif not last:
                            project(g, n + 1, 1 - q, 0, c)
                    transposes(s)
                    if not last:
                        values(g, n + 1, 1 - q, h)
                    attend(n, q, h, s)
                    if not first:
                        project_out(g, n - 1, 1 - q, h)

            pe.sem_inc(o_done, ONE)
            pe.wait_ge(const_in, 64)
            with pe.Fori(0, G) as g:
                project(g, B * g, 0, 0, 0)
                project(g, B * g, 0, 0, 1)
                for t in range(TT):
                    values(g, B * g, 0, t)
                row(g, B * g, 0, first=True)
                with pe.Fori(0, (B - 2) // 2) as i:
                    row(g, B * g + 2 * i + 1, 1)
                    row(g, B * g + 2 * i + 2, 0)
                row(g, B * g + (B - 1), 1, last=True)
                for t in range(TT):
                    project_out(g, B * g + (B - 1), 1, t)

        @block.scalar
        def _(act):
            def split_w(g, u, free=None, count=0):
                if free is not None:
                    act.wait_ge(free, count)
                act.wait_ge(w_in[u % 2], UNITS * 8 * g + 16 * (u // 2 + 1))
                nc.scalar.activation(w_part(u, HI), w_stage[:, u % 2], ACT.Copy).then_inc(w_hi, 1)

            def swap_halves(c, s):
                act.wait_ge(qk_done[c], s + 1)
                nc.scalar.activation(swap[0:ROT, c], p_qk[c][ROT:2 * ROT, :], ACT.Copy)
                nc.scalar.activation(swap[ROT:2 * ROT, c], p_qk[c][0:ROT, :], ACT.Copy).then_inc(qk_swap[c], 1)

            def split_qk(c, s):
                act.wait_ge(qk_rope[c], s + 1)
                nc.scalar.activation(qk[:, c, HI], p_qk[c][:], ACT.Copy).then_inc(qk_hi[c], 1)

            def exps(s):
                for r, i in enumerate(ORDER):
                    act.wait_ge(max_done, TT * s + r + 1)
                    cols = score_cols(i)
                    nc.scalar.activation(probs[:, cols], probs[:, cols], ACT.Exp, bias=neg_max[:, r:r + 1],
                                         scale=-1.0, accum_out=row_sum[:, r:r + 1]).then_inc(exp_done, 1)

            def split_probs(s):
                for bank, width in enumerate(BANK_WIDTH):
                    act.wait_ge(pt_done, 3 * s + bank + 1)
                    cols = slice(BANK_START[bank], BANK_START[bank] + width)
                    nc.scalar.activation(probs_t[:, HI, cols], p_sc[bank][:, 0:width], ACT.Copy).then_inc(pt_hi, 1)

            def split_v(n, q, t):
                act.wait_ge(v_done, TT * n + t + 1)
                nc.scalar.activation(v[:, q, HI, t], p_v[:], ACT.Copy).then_inc(v_hi, 1)

            def split_y(q, h, s):
                act.wait_ge(y_done, s + 1)
                nc.scalar.activation(y[:, q, HI, h], p_y[:], ACT.Copy).then_inc(y_hi, 1)

            def row(g, n, q, first=False, last=False):
                for h in range(HG):
                    s = HG * n + h
                    more = not (last and h == HG - 1)
                    exps(s)
                    if more:
                        swap_halves(0, s + 1)
                        split_qk(0, s + 1)
                    split_probs(s)
                    if more:
                        swap_halves(1, s + 1)
                    if not last:
                        split_v(n + 1, 1 - q, h)
                    if more:
                        split_qk(1, s + 1)
                    split_y(q, h, s)
                    if first:
                        split_w(g, KD + 2 * HG + h, o_done, HG * B * g + ONE)
                    if last:
                        for u in LOAD_AT[h]:
                            if u < KD:
                                split_w(g + 1, u, v_done, TT * B * (g + 1))
                            else:
                                split_w(g + 1, u, qk_done[1], HG * B * g + (HG * (B - 1) + (u - KD) // 2 + 1))

            for u in range(KD + 2 * HG):
                split_w(0, u)
            with act.Fori(0, G) as g:
                for c in range(2):
                    swap_halves(c, HG * B * g)
                    split_qk(c, HG * B * g)
                for t in range(TT):
                    split_v(B * g, 0, t)
                row(g, B * g, 0, first=True)
                with act.Fori(0, (B - 2) // 2) as i:
                    row(g, B * g + 2 * i + 1, 1)
                    row(g, B * g + 2 * i + 2, 0)
                row(g, B * g + (B - 1), 1, last=True)

        @block.gpsimd
        def _(pool):
            def split_w(g, u):
                pool.wait_ge(w_hi, UNITS * g + u + 1)
                nc.gpsimd.tensor_tensor(w_part(u, LO), w_stage[:, u % 2], w_part(u, HI).bitcast(F32),
                                        ALU.subtract).then_inc(w_lo, 1)

            def normalise(s):
                for r, i in enumerate(ORDER):
                    if r % 2 == 0:
                        wait_alone(pool, inv_done, 2 * s + r // 2 + 1, pool_passed)
                    cols = score_cols(i)
                    nc.gpsimd.tensor_scalar(probs[:, cols], probs[:, cols], inv_sum[:, r:r + 1], 1.0,
                                            ALU.mult, ALU.mult).then_inc(prob_done, 1)

            def times_sin(c, s):
                pool.wait_ge(qk_swap[c], s + 1)
                nc.gpsimd.tensor_tensor(swap[:, c], swap[:, c], sin[:], ALU.mult).then_inc(qk_sin[c], 1)

            def row(g, n, q, first=False, last=False):
                for h in range(HG):
                    s = HG * n + h
                    normalise(s)
                    if not (last and h == HG - 1):
                        times_sin(0, s + 1)
                        times_sin(1, s + 1)
                    if first:
                        split_w(g, KD + 2 * HG + h)
                    if last:
                        for u in LOAD_AT[h]:
                            split_w(g + 1, u)

            for u in range(KD + 2 * HG):
                split_w(0, u)
            pool.wait_ge(const_in, 64)
            with pool.Fori(0, G) as g:
                times_sin(0, HG * B * g)
                times_sin(1, HG * B * g)
                row(g, B * g, 0, first=True)
                with pool.Fori(0, (B - 2) // 2) as i:
                    row(g, B * g + 2 * i + 1, 1)
                    row(g, B * g + 2 * i + 2, 0)
                row(g, B * g + (B - 1), 1, last=True)

        @block.vector
        def _(dve):
            def masked_max(s):
                for bank, tiles in enumerate(SCORE_ORDER):
                    wait_alone(dve, score_done, 3 * s + bank + 1, dve_passed)
                    for i in tiles:
                        _, at, width = SCORE_AT[i]
                        r = ORDER.index(i)
                        nc.vector.tensor_tensor_reduce(
                            out=probs[:, score_cols(i)], in0=p_sc[bank][:, at:at + width],
                            in1=mask[:, T - width:], scale=-SCALE, scalar=3.0e38, op0=ALU.add, op1=ALU.min,
                            accum_out=neg_max[:, r:r + 1]).then_inc(max_done, 1)

            def invert(s):
                for r in range(2):
                    dve.wait_ge(exp_done, TT * s + 2 * r + 2)
                    nc.vector.reciprocal(inv_sum[:, 2 * r:2 * r + 2],
                                         row_sum[:, 2 * r:2 * r + 2]).then_inc(inv_done, 1)

            def times_cos(c, s):
                dve.wait_ge(qk_swap[c], s + 1)
                nc.vector.tensor_tensor(p_qk[c][0:2 * ROT, :], p_qk[c][0:2 * ROT, :], cos[:],
                                        ALU.mult).then_inc(qk_cos[c], 1)

            def rope(c, s):
                dve.wait_ge(qk_cos[c], s + 1)
                dve.wait_ge(qk_sin[c], s + 1)
                nc.vector.tensor_tensor(p_qk[c][0:2 * ROT, :], p_qk[c][0:2 * ROT, :], swap[:, c],
                                        ALU.add).then_inc(qk_rope[c], 1)

            def rest(to, bank, hi, signal):
                nc.vector.tensor_tensor(to, bank, hi.bitcast(F32), ALU.subtract).then_inc(signal, 1)

            def split_qk(c, s):
                dve.wait_ge(qk_hi[c], s + 1)
                rest(qk[:, c, LO], p_qk[c][:], qk[:, c, HI], qk_lo[c])

            def split_probs(s):
                for bank, width in enumerate(BANK_WIDTH):
                    dve.wait_ge(pt_hi, 3 * s + bank + 1)
                    cols = slice(BANK_START[bank], BANK_START[bank] + width)
                    rest(probs_t[:, LO, cols], p_sc[bank][:, 0:width], probs_t[:, HI, cols], pt_lo)

            def split_v(n, q, t):
                dve.wait_ge(v_hi, TT * n + t + 1)
                rest(v[:, q, LO, t], p_v[:], v[:, q, HI, t], v_lo)

            def split_y(q, h, s):
                dve.wait_ge(y_hi, s + 1)
                rest(y[:, q, LO, h], p_y[:], y[:, q, HI, h], y_lo)

            def add_out(n, t):
                dve.wait_ge(acc_in[t], 16 * n + 16)
                dve.wait_ge(o_done, TT * n + t + 1 + ONE)
                nc.vector.scalar_tensor_tensor(acc[:, t], p_o[:], 1.0 / 3.0, acc[:, t],
                                               ALU.mult, ALU.add).then_inc(acc_done, 1)

            def row(g, n, q, first=False, last=False):
                for h in range(HG):
                    s = HG * n + h
                    more = not (last and h == HG - 1)
                    masked_max(s)
                    invert(s)
                    if more:
                        times_cos(0, s + 1)
                        rope(0, s + 1)
                        split_qk(0, s + 1)
                    split_probs(s)
                    if more:
                        times_cos(1, s + 1)
                    if not last:
                        split_v(n + 1, 1 - q, h)
                    if more:
                        rope(1, s + 1)
                        split_qk(1, s + 1)
                    split_y(q, h, s)
                    if not first:
                        add_out(n - 1, h)

            for counted in (v_lo, y_lo, acc_done):
                dve.sem_inc(counted, ONE)
            dve.wait_ge(const_in, 64)
            with dve.Fori(0, G) as g:
                for c in range(2):
                    times_cos(c, HG * B * g)
                    rope(c, HG * B * g)
                    split_qk(c, HG * B * g)
                for t in range(TT):
                    split_v(B * g, 0, t)
                row(g, B * g, 0, first=True)
                with dve.Fori(0, (B - 2) // 2) as i:
                    row(g, B * g + 2 * i + 1, 1)
                    row(g, B * g + 2 * i + 2, 0)
                row(g, B * g + (B - 1), 1, last=True)
                for t in range(TT):
                    add_out(B * g + (B - 1), t)


def build(nc, x, ffnw, ffns, down_s, wqk, wv, wo, const, out):
    xt_dram = nc.dram_tensor("xt_split", (B, P, 2, KD, T), F32, kind="Internal").ap()
    x_tiles = x.rearrange("b (t p) d -> b p t d", p=P)
    out_tiles = out.rearrange("b (t p) d -> b p t d", p=P)
    ffn_phase(nc, x_tiles, ffnw, ffns, down_s, const, xt_dram, out_tiles)
    attention_phase(nc, wqk, wv, wo, const, xt_dram, out_tiles)


def constants(np):
    table = np.zeros((P, 3 * T + P), np.float32)
    table[:, C_MASK + T - P:C_MASK + T] = np.triu(np.full((P, P), -1e30, np.float32), 1)
    table[:, C_IDENT:C_IDENT + P] = np.eye(P, dtype=np.float32)
    freq = np.float32(1.0 / 1024.0) ** np.linspace(0.0, 1.0, ROT, dtype=np.float32)
    angle = freq[:, None] * np.arange(T, dtype=np.float32)[None, :]
    table[0:ROT, C_COS:C_COS + T] = table[ROT:2 * ROT, C_COS:C_COS + T] = np.cos(angle)
    table[0:ROT, C_SIN:C_SIN + T] = np.sin(angle)
    table[ROT:2 * ROT, C_SIN:C_SIN + T] = -np.sin(angle)
    return table


def kernel(L0_attn_x, L0_attn_Wq, L0_attn_Wk, L0_attn_Wv, L0_attn_Wo, L0_ffn_gate_w, L0_ffn_up_w,
           L0_ffn_down_w, L0_ffn_gate_s, L0_ffn_up_s, L0_ffn_down_s):
    import numpy as np
    import concourse.bacc as bacc
    from concourse.bass_utils import run_bass_kernel_spmd

    def tiles(w):
        return np.asarray(w).T.reshape(KD, P, -1).transpose(1, 0, 2)

    order = np.r_[0:ROT, DH // 2:DH // 2 + ROT, ROT:DH // 2, DH // 2 + ROT:DH]
    wqk = np.stack([tiles(w).reshape(P, KD, G, HG, DH)[..., order].transpose(2, 3, 0, 1, 4)
                    for w in (L0_attn_Wq, L0_attn_Wk)], axis=2)
    wv = tiles(L0_attn_Wv).reshape(P, KD, G, HG * DH).transpose(2, 1, 0, 3)
    wo = np.asarray(L0_attn_Wo).T.reshape(G, HG, P, D)
    gate_up = [tiles(w).reshape(P, KD, J, P).transpose(2, 0, 1, 3).reshape(J, P, KD * P)
               for w in (L0_ffn_gate_w, L0_ffn_up_w)]
    ffnw = np.stack([*gate_up, np.asarray(L0_ffn_down_w).T.reshape(J, P, D)], axis=1)
    arrays = {
        "x": np.asarray(L0_attn_x),
        "ffnw": ffnw.reshape(3 * J, P, 512),
        "ffns": np.stack([np.asarray(s).reshape(J, P).T for s in (L0_ffn_gate_s, L0_ffn_up_s)], axis=1),
        "down_s": np.broadcast_to(np.asarray(L0_ffn_down_s), (P, D)),
        "wqk": wqk.reshape(G, 2 * HG, P, KD * DH),
        "wv": wv,
        "wo": wo,
        "const": constants(np),
    }
    arrays = {f"in_{name}": np.ascontiguousarray(a) for name, a in arrays.items()}
    nc = bacc.Bacc("TRN2", target_bir_lowering=False, num_devices=1)
    args = [nc.dram_tensor(name, a.shape, mybir.dt.from_np(a.dtype), kind="ExternalInput").ap()
            for name, a in arrays.items()]
    out = nc.dram_tensor("out", (B, T, D), F32, kind="ExternalOutput").ap()
    build(nc, *args, out)
    return run_bass_kernel_spmd(nc, [arrays], core_ids=[0]).results[0]["out"]
```

```python
from contextlib import ExitStack

import concourse.bass as bass
from concourse import mybir

ALU = mybir.AluOpType
ACT = mybir.ActivationFunctionType
F32 = mybir.dt.float32
F32R = mybir.dt.float32r
I32 = mybir.dt.int32
AX_X = mybir.AxisListType.X

P = 128
B = 8
T = 512
D = 512
H = 16
DH = 128
INTER = 1408
TT = T // P
KD = D // P
J = INTER // P
HG = 4
G = H // HG
ROT = DH // 4
EPS = 1e-5
SCALE = float(DH) ** 0.5 / DH
HI, LO = 0, 1
NEXT = 5

SCORE_AT = {3: (0, 0, 512), 2: (1, 0, 384), 0: (1, 384, 128), 1: (2, 0, 256)}
SCORE_ORDER = [[3], [2, 0], [1]]
PROB_AT = {j: SCORE_AT[TT - 1 - j] for j in range(TT)}
BANK_WIDTH = [512, 512, 256]
BANK_START = [0, 512, 1024]
CAUSAL = sum(BANK_WIDTH)

C_MASK, C_IDENT, C_COS, C_SIN = 0, T, T + P, 2 * T + P


def wait_alone(eng, sem, count, passed):
    eng.wait_ge(sem, count)
    eng.sem_inc(passed, 1)


def products(pe, out, w, x, start, stop, w_lo=True, x_lo=True):
    passes = [(LO, HI)] * w_lo + [(HI, LO)] * x_lo + [(HI, HI)]
    for i, (a, b) in enumerate(passes):
        mm = pe.matmul(out, w(a), x(b), start=start and i == 0, stop=stop and i == len(passes) - 1)
    return mm


def ffn_phase(nc, xt, x_in_next, stage, w_in_next, wqk_dram, x_dram, ffnw_dram, ffns_dram, down_dram, const_dram, xt_dram, out):
    with ExitStack() as ctx:
        def sb(name, shape, dt=F32):
            return ctx.enter_context(nc.sbuf_tensor(name, shape, dt))

        def ps(name, shape):
            return ctx.enter_context(nc.psum_tensor(name, shape, F32))

        def sem(name):
            return ctx.enter_context(nc.semaphore(name))

        w = sb("ffn_w", [P, 2, J, 3, 512], F32R)
        stage_2 = sb("ffn_w_stage", [P, 512])
        xin = sb("ffn_xin", [P, 2, TT, D])
        xn = sb("ffn_xn", [P, 2, D])
        hid = sb("ffn_hid", [P, 2, 2, T], F32R)
        silu = sb("ffn_silu", [P, T])
        down_s = sb("ffn_down_s", [P, D])
        ident = sb("ffn_ident", [P, P])
        gu_s = sb("ffn_gu_s", [P, 2, J])
        stats = sb("ffn_stats", [P, TT, 6])
        mv = sb("ffn_mv", [P, TT, 2])
        veps = sb("ffn_veps", [P, TT])
        rstd = sb("ffn_rstd", [P, TT])
        half = sb("ffn_half", [P, TT])
        ones = sb("ffn_ones", [P, 1])
        lo_max = sb("ffn_lo_max", [P, J + 1])
        lo_any = sb("ffn_lo_any", [P, 1])
        lo_count = sb("ffn_lo_count", [1, 1], I32)

        p_gate = ps("p_gate", [P, T])
        p_up = ps("p_up", [P, T])
        p_tr = [ps(f"p_tr{i}", [P, KD, P]) for i in range(2)]
        p_down = [ps(f"p_down{t}", [P, D]) for t in range(TT)]

        const_in = sem("f_const_in")
        down_s_in = sem("f_down_s_in")
        half_set = sem("f_half_set")
        ones_set = sem("f_ones_set")
        lo_max_done = sem("f_lo_max_done")
        lo_any_done = sem("f_lo_any_done")
        lo_summed = sem("f_lo_summed")
        lo_counted = sem("f_lo_counted")
        w_stage = [stage[:, 0], stage[:, 1], stage_2[:]]
        x_in = [sem(f"f_x_in{i}") for i in range(2)]
        w_in = [sem(f"f_w_in{i}") for i in range(3)]
        w_hi = sem("f_w_hi")
        w_lo = sem("f_w_lo")
        st = sem("f_stats")
        passed = sem("f_passed")
        ag = sem("f_aggr")
        ve = sem("f_veps")
        rs = sem("f_rstd")
        xn_done = sem("f_xn")
        tr_done = sem("f_tr")
        tr_hi = sem("f_tr_hi")
        tr_lo = sem("f_tr_lo")
        gate_done = sem("f_gate")
        up_done = sem("f_up")
        silu_done = sem("f_silu")
        hid_done = sem("f_hid")
        hid_hi = sem("f_hid_hi")
        hid_lo = sem("f_hid_lo")
        down_done = sem("f_down")
        scaled = sem("f_scaled")
        sum_done = sem("f_sum")
        xt_out = sem("f_xt_out")
        sum_out = sem("f_sum_out")
        block = ctx.enter_context(nc.Block())

        @block.sync
        def _(sp):
            sp.dma_start(xin[:, 0], x_dram[0]).then_inc(x_in[0], 16)
            sp.dma_start(ident[:], const_dram[:, C_IDENT:C_IDENT + P]).then_inc(const_in, 16)
            sp.dma_start(gu_s[:], ffns_dram).then_inc(const_in, 16)
            for u in range(3 * J):
                if u >= 3:
                    sp.wait_ge(w_lo, u - 2)
                sp.dma_start(w_stage[u % 3], ffnw_dram[u]).then_inc(w_in[u % 3], 16)
                if u == 3:
                    sp.dma_start(down_s[:], down_dram).then_inc(down_s_in, 16)
                    sp.dma_start(xin[:, 1], x_dram[1]).then_inc(x_in[1], 16)

            def row(b, q, last=False):
                sp.wait_ge(xt_out, 16 * b)
                sp.wait_ge(tr_lo, TT * b + TT)
                sp.dma_start(xt_dram[b], xt[:, q].bitcast(F32)).then_inc(xt_out, 16)
                if last:
                    sp.wait_ge(up_done, J * b)
                    sp.dma_start(xt[:, 1 - q].bitcast(F32), xt_dram[0]).then_inc(x_in_next, 16)
                    sp.wait_ge(w_lo, 3 * J)
                    for c in range(2):
                        sp.dma_start(stage[:, c], wqk_dram[0, c]).then_inc(w_in_next[c], 16)
                if last:
                    for t in range(TT):
                        sp.wait_ge(sum_done, TT * b + t + 1)
                        sp.dma_start(out[b, :, t], xin[:, q, t]).then_inc(sum_out, 16)
                else:
                    sp.wait_ge(sum_done, TT * b + TT)
                    sp.dma_start(out[b], xin[:, q]).then_inc(sum_out, 16)

            def load(b, q):
                sp.wait_ge(sum_out, 16 * b - 16)
                sp.dma_start(xin[:, q], x_dram[b]).then_inc(x_in[q], 16)

            row(0, 0)
            with sp.Fori(0, (B - 2) // 2) as i:
                load(2 * i + 2, 0)
                row(2 * i + 1, 1)
                load(2 * i + 3, 1)
                row(2 * i + 2, 0)
            row(B - 1, 1, last=True)
            sp.wait_ge(xt_out, 16 * B)
            sp.wait_ge(sum_out, 16 * (B - 1 + TT))

        @block.tensor
        def _(pe):
            def transposes(b, q, t):
                pe.wait_ge(xn_done, TT * b + t + 1)
                if t >= 2:
                    pe.wait_ge(tr_lo, TT * b + t - 1)
                for k in range(KD):
                    mm = pe.transpose(p_tr[t % 2][:, k], xn[:, t % 2, k * P:(k + 1) * P], ident[:])
                mm.then_inc(tr_done, 1)

            def gate_up(b, q, j, full):
                pe.wait_ge(w_lo, 3 * j + 2)
                if j == 0:
                    pe.wait_ge(tr_lo, TT * b + TT)
                for out_, c, ready, done in ((p_gate, 0, silu_done, gate_done), (p_up, 1, hid_lo, up_done)):
                    pe.wait_ge(ready, J * b + j)
                    for k in range(KD):
                        mm = products(pe, out_[:], lambda h: w[:, h, j, c, k * P:(k + 1) * P],
                                      lambda h: xt[:, q, h, k], k == 0, k == KD - 1, w_lo=full)
                    mm.then_inc(done, 1)

            def down(b, q, j, full):
                pe.wait_ge(w_lo, 3 * j + 3)
                pe.wait_ge(hid_lo, J * b + j + 1)
                r = (q + j) % 2
                for t in range(TT):
                    if j == 0 and (not isinstance(b, int) or b):
                        pe.wait_ge(sum_done, TT * b - TT + t + 1)
                    mm = products(pe, p_down[t][:], lambda h: hid[:, r, h, t * P:(t + 1) * P],
                                  lambda h: w[:, h, j, 2], j == 0, j == J - 1, x_lo=full)
                mm.then_inc(down_done, 1)

            def count_low_parts():
                pe.wait_ge(ones_set, 1)
                pe.wait_ge(lo_any_done, 1)
                pe.wait_ge(tr_lo, 2 * TT)
                pe.matmul(p_tr[0][0:1, 0, 0:1], lo_any[:], ones[:], start=True, stop=True).then_inc(lo_summed, 1)

            def row(b, q, full, first=False, last=False):
                for j in range(J):
                    gate_up(b, q, j, full)
                    if first and j == J - 1:
                        count_low_parts()
                    if j:
                        down(b, q, j - 1, full)
                    elif not first:
                        down(b - 1, 1 - q, J - 1, full)
                    if NEXT <= j < NEXT + TT and not last:
                        transposes(b + 1, 1 - q, j - NEXT)

            def other_rows(full):
                with pe.Fori(0, (B - 2) // 2) as i:
                    row(2 * i + 1, 1, full)
                    row(2 * i + 2, 0, full)
                row(B - 1, 1, full, last=True)
                down(B - 1, 1, J - 1, full)

            pe.wait_ge(const_in, 32)
            for t in range(TT):
                transposes(0, 0, t)
            row(0, 0, True, first=True)
            pe.wait_ge(lo_counted, 1)
            low_parts = pe.value_load(lo_count[0:1, 0:1], min_val=0, max_val=P)
            with pe.If(low_parts):
                other_rows(True)
            with pe.Else():
                other_rows(False)

        @block.scalar
        def _(act):
            def split_w(u):
                act.wait_ge(w_in[u % 3], 16 * (u // 3) + 16)
                nc.scalar.activation(w[:, HI, u // 3, u % 3], w_stage[u % 3], ACT.Copy).then_inc(w_hi, 1)

            def split_x(b, q, t):
                act.wait_ge(tr_done, TT * b + t + 1)
                nc.scalar.activation(xt[:, q, HI, :, t * P:(t + 1) * P], p_tr[t % 2][:],
                                     ACT.Copy).then_inc(tr_hi, 1)

            def hidden(b, q, j):
                act.wait_ge(gate_done, J * b + j + 1)
                act.wait_ge(hid_done, J * b + j)
                nc.scalar.activation(silu[:], p_gate[:], ACT.Silu,
                                     scale=gu_s[:, 0, j:j + 1]).then_inc(silu_done, 1)
                act.wait_ge(hid_done, J * b + j + 1)
                nc.scalar.activation(hid[:, (q + j) % 2, HI], p_up[:], ACT.Copy).then_inc(hid_hi, 1)

            def row(b, q, first=False, last=False):
                for j in range(J):
                    if first and j < J - 1:
                        for c in range(3):
                            split_w(3 * j + 3 + c)
                    hidden(b, q, j)
                    if j == NEXT and not last:
                        act.wait_ge(xt_out, 16 * b)
                    if NEXT <= j < NEXT + TT and not last:
                        split_x(b + 1, 1 - q, j - NEXT)

            act.wait_ge(const_in, 32)
            split_w(0)
            split_w(1)
            split_w(2)
            for t in range(TT):
                split_x(0, 0, t)
            row(0, 0, first=True)
            with act.Fori(0, (B - 2) // 2) as i:
                row(2 * i + 1, 1)
                row(2 * i + 2, 0)
            row(B - 1, 1, last=True)

        @block.gpsimd
        def _(pool):
            nc.gpsimd.memset(half[:], -0.5).then_inc(half_set, 1)
            nc.gpsimd.memset(ones[:], 1.0).then_inc(ones_set, 1)
            pool.wait_ge(half_set, 1)

            def split_w(u):
                pool.wait_ge(w_hi, u + 1)
                nc.gpsimd.tensor_tensor(w[:, LO, u // 3, u % 3], w_stage[u % 3],
                                        w[:, HI, u // 3, u % 3].bitcast(F32), ALU.subtract).then_inc(w_lo, 1)

            def root(b):
                pool.wait_ge(ve, b + 1)
                nc.gpsimd.tensor_tensor(rstd[:], veps[:], half[:], ALU.pow).then_inc(rs, 1)

            root(0)
            for u in range(3 * NEXT + 3):
                split_w(u)
            root(1)
            for u in range(3 * NEXT + 3, 3 * J):
                split_w(u)
            with pool.Fori(2, B) as b:
                root(b)

        @block.vector
        def _(dve):
            def statistics(b, q):
                dve.wait_ge(x_in[q], 8 * b + 16 - 8 * q)
                for t in range(TT):
                    ins = nc.vector.bn_stats(stats[:, t], xin[:, q, t])
                ins.then_inc(st, 1)
                wait_alone(dve, st, b + 1, passed)
                for t in range(TT):
                    ins = nc.vector.bn_aggr(mv[:, t], stats[:, t])
                ins.then_inc(ag, 1)
                dve.wait_ge(ag, b + 1)
                nc.vector.tensor_scalar(veps[:], mv[:, :, 1], EPS, None, ALU.add).then_inc(ve, 1)

            def normalise(b, q, t):
                dve.wait_ge(rs, b + 1)
                if t >= 2:
                    dve.wait_ge(tr_done, TT * b + t - 1)
                nc.vector.tensor_scalar(xn[:, t % 2], xin[:, q, t], mv[:, t, 0:1], rstd[:, t:t + 1],
                                        ALU.subtract, ALU.mult).then_inc(xn_done, 1)

            def split_x(b, q, t):
                dve.wait_ge(tr_hi, TT * b + t + 1)
                s = slice(t * P, (t + 1) * P)
                nc.vector.tensor_tensor(xt[:, q, LO, :, s], p_tr[t % 2][:], xt[:, q, HI, :, s].bitcast(F32),
                                        ALU.subtract).then_inc(tr_lo, 1)

            def hidden(b, q, j):
                dve.wait_ge(silu_done, J * b + j + 1)
                dve.wait_ge(up_done, J * b + j + 1)
                nc.vector.scalar_tensor_tensor(p_up[:], p_up[:], gu_s[:, 1, j:j + 1], silu[:],
                                               ALU.mult, ALU.mult).then_inc(hid_done, 1)
                dve.wait_ge(hid_hi, J * b + j + 1)
                r = (q + j) % 2
                nc.vector.tensor_tensor(hid[:, r, LO], p_up[:], hid[:, r, HI].bitcast(F32),
                                        ALU.subtract).then_inc(hid_lo, 1)

            def sums(b, q):
                dve.wait_ge(down_done, J * b + J)
                for i in range(TT + 1):
                    if i < TT:
                        nc.vector.tensor_tensor(p_down[i][:], p_down[i][:], down_s[:], ALU.mult).then_inc(scaled, 1)
                    if i:
                        t = i - 1
                        dve.wait_ge(scaled, TT * b + t + 1)
                        nc.vector.tensor_tensor(xin[:, q, t], p_down[t][:], xin[:, q, t],
                                                ALU.add).then_inc(sum_done, 1)

            def largest_low_part(j):
                dve.wait_ge(w_lo, 3 * j + 3)
                nc.vector.reduce_max(lo_max[:, j:j + 1], w[:, LO, j].bitcast(F32).rearrange("p c n -> p (c n)"),
                                     axis=AX_X, apply_absolute_value=True).then_inc(lo_max_done, 1)

            def any_low_part():
                dve.wait_ge(lo_max_done, J)
                nc.vector.reduce_max(lo_max[:, J:J + 1], lo_max[:, 0:J], axis=AX_X).then_inc(lo_max_done, 1)
                dve.wait_ge(lo_max_done, J + 1)
                nc.vector.tensor_scalar(lo_any[:], lo_max[:, J:J + 1], 0.0, None, ALU.is_gt).then_inc(lo_any_done, 1)

            def count_low_parts():
                dve.wait_ge(lo_summed, 1)
                nc.vector.tensor_copy(lo_count[:], p_tr[0][0:1, 0, 0:1]).then_inc(lo_counted, 1)

            def row(b, q, first=False, last=False):
                for j in range(J):
                    hidden(b, q, j)
                    if first and j < J - 1:
                        largest_low_part(j)
                    if first and j == J - 2:
                        largest_low_part(J - 1)
                        any_low_part()
                    if first and j == J - 1:
                        count_low_parts()
                    if j == 0 and not first:
                        sums(b - 1, 1 - q)
                    if last:
                        continue
                    if j == NEXT - 1:
                        statistics(b + 1, 1 - q)
                        normalise(b + 1, 1 - q, 0)
                        normalise(b + 1, 1 - q, 1)
                    if NEXT <= j < NEXT + TT:
                        split_x(b + 1, 1 - q, j - NEXT)
                        if j - NEXT + 2 < TT:
                            normalise(b + 1, 1 - q, j - NEXT + 2)

            statistics(0, 0)
            normalise(0, 0, 0)
            normalise(0, 0, 1)
            for t in range(TT):
                split_x(0, 0, t)
                if t < 2:
                    normalise(0, 0, t + 2)
            dve.wait_ge(const_in, 32)
            dve.wait_ge(down_s_in, 16)
            row(0, 0, first=True)
            with dve.Fori(0, (B - 2) // 2) as i:
                row(2 * i + 1, 1)
                row(2 * i + 2, 0)
            row(B - 1, 1, last=True)
            sums(B - 1, 1)


def attention_phase(nc, xt, x_in, w_stage, first_in, wqk_dram, wv_dram, wo_dram, const_dram, xt_dram, out):
    with ExitStack() as ctx:
        def sb(name, shape, dt=F32):
            return ctx.enter_context(nc.sbuf_tensor(name, shape, dt))

        def ps(name, shape):
            return ctx.enter_context(nc.psum_tensor(name, shape, F32))

        def sem(name):
            return ctx.enter_context(nc.semaphore(name))

        w_qk = sb("w_qk", [P, 2, HG, 2, KD, DH], F32R)
        w_v = sb("w_v", [P, 2, KD, HG * DH], F32R)
        w_o = sb("w_o", [P, 2, HG, D], F32R)
        v = sb("v", [P, 2, 2, TT, HG * DH], F32R)
        y = sb("y", [P, 2, 2, HG, T], F32R)
        qk = sb("qk", [P, 2, 2, T], F32R)
        probs = sb("probs", [P, CAUSAL])
        probs_t = sb("probs_t", [P, 2, CAUSAL], F32R)
        swap = sb("swap", [2 * ROT, 2, T])
        mask = sb("mask", [P, T])
        ident = sb("ident", [P, P])
        cos = sb("cos", [2 * ROT, T])
        sin = sb("sin", [2 * ROT, T])
        acc = sb("acc", [P, TT, D])
        neg_max = sb("neg_max", [P, TT])
        row_sum = sb("row_sum", [P, TT])
        inv_sum = sb("inv_sum", [P, TT])

        p_sc = [ps(f"p_sc{i}", [P, 512]) for i in range(3)]
        p_qk = [ps("p_q", [P, T]), ps("p_k", [P, T])]
        p_v = ps("p_v", [P, HG * DH])
        p_y = ps("p_y", [P, T])
        p_o = ps("p_o", [P, D])

        const_in = sem("const_in")
        w_in = [sem(f"w_in{i}") for i in range(2)]
        first_in = [*first_in, *(sem(f"first_in{2 + t}") for t in range(TT))]
        w_hi = sem("w_hi")
        w_lo = sem("w_lo")
        qk_done = [sem("q_done"), sem("k_done")]
        qk_swap = [sem("q_swap"), sem("k_swap")]
        qk_sin = [sem("q_sin"), sem("k_sin")]
        qk_cos = [sem("q_cos"), sem("k_cos")]
        qk_rope = [sem("q_rope"), sem("k_rope")]
        qk_hi = [sem("q_hi"), sem("k_hi")]
        qk_lo = [sem("q_lo"), sem("k_lo")]
        v_done = sem("v_done")
        v_hi = sem("v_hi")
        v_lo = sem("v_lo")
        score_done = sem("score_done")
        dve_passed = sem("dve_passed")
        pool_passed = sem("pool_passed")
        max_done = sem("max_done")
        exp_done = sem("exp_done")
        inv_done = sem("inv_done")
        prob_done = sem("prob_done")
        pt_done = sem("pt_done")
        pt_hi = sem("pt_hi")
        pt_lo = sem("pt_lo")
        y_done = sem("y_done")
        y_hi = sem("y_hi")
        y_lo = sem("y_lo")
        o_done = sem("o_done")
        acc_in = [sem(f"acc_in{t}") for t in range(TT)]
        acc_done = sem("acc_done")
        acc_out = [sem(f"acc_out{t}") for t in range(TT)]
        block = ctx.enter_context(nc.Block())

        ONE = 1
        UNITS = 4 * HG
        LOAD_AT = {0: [0, 1, 2], 1: [3, 4, 5], 2: [6, 7, 8, 9], 3: [10, 11]}
        QK_UNIT = [0] + [KD + 2 * h for h in range(1, HG)]
        V_UNIT, O_UNIT = 2, KD + 2 * HG

        first_stage = [w_stage[:, 0], w_stage[:, 1], *(acc[:, t] for t in range(TT))]
        STAGES = len(first_stage)

        def kind(u):
            for h in range(HG):
                if u - QK_UNIT[h] in (0, 1):
                    return "qk", h
            return ("v", u - V_UNIT) if u < O_UNIT else ("o", u - O_UNIT)

        def w_part(u, part):
            what, i = kind(u)
            if what == "qk":
                return w_qk[:, part, i, u - QK_UNIT[i]]
            return w_v[:, part, i] if what == "v" else w_o[:, part, i]

        @block.sync
        def _(sp):
            def load_unit(g, u, first=False):
                gw = 0 if first else sp.snap(g % G)
                if not first:
                    sp.wait_ge(w_lo, g * UNITS + (u - 1))
                elif u >= STAGES:
                    sp.wait_ge(w_lo, u - STAGES + 1)
                what, i = kind(u)
                if what == "qk":
                    src = wqk_dram[gw, 2 * i + u - QK_UNIT[i]]
                else:
                    src = (wv_dram if what == "v" else wo_dram)[gw, i]
                if first:
                    sp.dma_start(first_stage[u % STAGES], src).then_inc(first_in[u % STAGES], 16)
                else:
                    sp.dma_start(w_stage[:, u % 2], src).then_inc(w_in[u % 2], 16)

            def load_acc(b, n, t):
                sp.wait_ge(acc_out[t], 16 * n + ONE)
                sp.dma_start(acc[:, t], out[b, :, t]).then_inc(acc_in[t], 16)

            def store_acc(b, n, t):
                sp.wait_ge(acc_done, TT * n + t + 1 + ONE)
                sp.dma_start(out[b, :, t], acc[:, t]).then_inc(acc_out[t], 16)

            def load_x(b, n, q):
                sp.wait_ge(qk_done[1], HG * n - HG)
                sp.dma_start(xt[:, q].bitcast(F32), xt_dram[b]).then_inc(x_in[q], 16)

            def row(g, n, q, first=False, last=False, b=None):
                for h in range(HG):
                    if first:
                        load_unit(g, O_UNIT + h)
                    if not first:
                        load_acc(b - 1, n - 1, h)
                        if h:
                            store_acc(b - 1, n - 1, h - 1)
                    if last:
                        for u in LOAD_AT[h]:
                            load_unit(g + 1, u)
                    if h == HG - 1:
                        load_x((b + 2) % B if isinstance(b, int) else b + 2, n + 2, q)
                if not first:
                    store_acc(b - 1, n - 1, HG - 1)

            for t in range(TT):
                sp.sem_inc(acc_out[t], ONE)
            for u in range(2, O_UNIT):
                load_unit(0, u, first=True)
                if u == V_UNIT + KD - 1:
                    for dst, at in ((mask, C_MASK), (ident, C_IDENT), (cos, C_COS), (sin, C_SIN)):
                        rows_, width = dst.shape
                        sp.dma_start(dst[:], const_dram[0:rows_, at:at + width]).then_inc(const_in, 16)
            sp.dma_start(xt[:, 1].bitcast(F32), xt_dram[1]).then_inc(x_in[1], 16)
            with sp.Fori(0, G) as g:
                row(g, g * B, 0, first=True, b=0)
                with sp.Fori(0, (B - 4) // 2) as i:
                    row(g, g * B + 2 * i + 1, 1, b=2 * i + 1)
                    row(g, g * B + 2 * i + 2, 0, b=2 * i + 2)
                row(g, g * B + (B - 3), 1, b=B - 3)
                row(g, g * B + (B - 2), 0, b=B - 2)
                row(g, g * B + (B - 1), 1, last=True, b=B - 1)
                for t in range(TT):
                    load_acc(B - 1, g * B + (B - 1), t)
                for t in range(TT):
                    store_acc(B - 1, g * B + (B - 1), t)
            for t in range(TT):
                sp.wait_ge(acc_out[t], 16 * G * B + ONE)
            for i in range(2):
                sp.wait_ge(x_in[i], 16 * (G * B // 2 + 1))

        ORDER = [i for tiles in SCORE_ORDER for i in tiles]

        def score_cols(i):
            bank, at, width = SCORE_AT[i]
            return slice(BANK_START[bank] + at, BANK_START[bank] + at + width)

        @block.tensor
        def _(pe):
            def project(g, n, q, h, c):
                pe.wait_ge(w_lo, UNITS * g + (QK_UNIT[h] + c + 1))
                pe.wait_ge(x_in[q], 8 * n + 16 - 8 * q)
                for k in range(KD):
                    mm = products(pe, p_qk[c][:], lambda a: w_qk[:, a, h, c, k],
                                  lambda a: xt[:, q, a, k], k == 0, k == KD - 1)
                mm.then_inc(qk_done[c], 1)

            def values(g, n, q, t, edge=False):
                pe.wait_ge(x_in[q], 8 * n + 16 - 8 * q)
                pe.wait_ge(v_lo, TT * n + (max(t - 1, 0) if edge else t) + ONE)
                if edge and t == 1:
                    pe.wait_ge(acc_done, TT * n + ONE)
                bank = p_y if edge and t % 2 == 0 else p_v
                for k in range(KD):
                    if edge and t == 0:
                        pe.wait_ge(w_lo, UNITS * g + (V_UNIT + k + 1))
                    mm = products(pe, bank[:], lambda a: xt[:, q, a, k, t * P:(t + 1) * P],
                                  lambda a: w_v[:, a, k], k == 0, k == KD - 1)
                mm.then_inc(v_done, 1)

            def scores(s):
                pe.wait_ge(qk_lo[0], s + 1)
                pe.wait_ge(qk_lo[1], s + 1)
                for bank, tiles in enumerate(SCORE_ORDER):
                    for i in tiles:
                        _, at, width = SCORE_AT[i]
                        mm = products(pe, p_sc[bank][:, at:at + width],
                                      lambda a: qk[:, 0, a, i * P:(i + 1) * P],
                                      lambda a: qk[:, 1, a, 0:width], True, True)
                    mm.then_inc(score_done, 1)

            def transposes(s):
                pe.wait_ge(prob_done, TT * s + TT)
                for bank, tiles in enumerate(SCORE_ORDER):
                    for j in [TT - 1 - i for i in tiles]:
                        _, at, width = PROB_AT[j]
                        for i in range(j, TT):
                            block_at = score_cols(i).start + j * P
                            to = at + (i - j) * P
                            mm = pe.transpose(p_sc[bank][:, to:to + P], probs[:, block_at:block_at + P], ident[:])
                    mm.then_inc(pt_done, 1)

            def attend(n, q, h, s):
                pe.wait_ge(v_lo, TT * n + TT + ONE)
                pe.wait_ge(y_lo, s + ONE)
                for bank, tiles in enumerate(SCORE_ORDER):
                    pe.wait_ge(pt_lo, 3 * s + (bank + 1))
                    for j in [TT - 1 - i for i in tiles]:
                        _, at, width = PROB_AT[j]
                        cols = slice(BANK_START[bank] + at, BANK_START[bank] + at + width)
                        mm = products(pe, p_y[:, j * P:], lambda a: v[:, q, a, j, h * DH:(h + 1) * DH],
                                      lambda a: probs_t[:, a, cols], j == 0, j == TT - 1 - ORDER[-1])
                mm.then_inc(y_done, 1)

            def project_out(g, n, q, t, edge=False):
                pe.wait_ge(w_lo, UNITS * g + UNITS)
                early = edge and t == 0
                pe.wait_ge(y_lo, HG * n + HG - early + ONE)
                if not early:
                    pe.wait_ge(acc_done, TT * n + (t - 1 if edge else t) + ONE)
                bank = p_v if edge and t % 2 == 0 else p_o
                for h in range(HG):
                    if early and h == HG - 1:
                        pe.wait_ge(y_lo, HG * n + HG + ONE)
                    mm = products(pe, bank[:], lambda a: y[:, q, a, h, t * P:(t + 1) * P],
                                  lambda a: w_o[:, a, h], h == 0, h == HG - 1)
                mm.then_inc(o_done, 1)

            def row(g, n, q, first=False, last=False):
                for h in range(HG):
                    s = HG * n + h
                    scores(s)
                    for c in range(2):
                        if h < HG - 1:
                            project(g, n, q, h + 1, c)
                        else:
                            project(g + 1 if last else g, n + 1, 1 - q, 0, c)
                    transposes(s)
                    if not last:
                        values(g, n + 1, 1 - q, h)
                    else:
                        project_out(g, n - 1, 1 - q, h)
                    attend(n, q, h, s)
                    if not first and not last:
                        project_out(g, n - 1, 1 - q, h)

            pe.sem_inc(o_done, ONE)
            pe.wait_ge(const_in, 64)
            project(0, 0, 0, 0, 0)
            project(0, 0, 0, 0, 1)
            with pe.Fori(0, G) as g:
                for t in range(TT):
                    values(g, B * g, 0, t, edge=True)
                row(g, B * g, 0, first=True)
                with pe.Fori(0, (B - 2) // 2) as i:
                    row(g, B * g + 2 * i + 1, 1)
                    row(g, B * g + 2 * i + 2, 0)
                row(g, B * g + (B - 1), 1, last=True)
                for t in range(TT):
                    project_out(g, B * g + (B - 1), 1, t, edge=True)

        @block.scalar
        def _(act):
            def split_w(g, u, free=None, count=0):
                if free is not None:
                    act.wait_ge(free, count)
                act.wait_ge(w_in[u % 2], UNITS * 8 * g + 16 * (u // 2 + 1 - O_UNIT // 2))
                nc.scalar.activation(w_part(u, HI), w_stage[:, u % 2], ACT.Copy).then_inc(w_hi, 1)

            def split_first_w(u):
                act.wait_ge(first_in[u % STAGES], 16 * (u // STAGES + 1))
                nc.scalar.activation(w_part(u, HI), first_stage[u % STAGES], ACT.Copy).then_inc(w_hi, 1)

            def swap_halves(c, s):
                act.wait_ge(qk_done[c], s + 1)
                nc.scalar.activation(swap[0:ROT, c], p_qk[c][ROT:2 * ROT, :], ACT.Copy)
                nc.scalar.activation(swap[ROT:2 * ROT, c], p_qk[c][0:ROT, :], ACT.Copy).then_inc(qk_swap[c], 1)

            def split_qk(c, s):
                act.wait_ge(qk_rope[c], s + 1)
                nc.scalar.activation(qk[:, c, HI], p_qk[c][:], ACT.Copy).then_inc(qk_hi[c], 1)

            def exps(s):
                for r, i in enumerate(ORDER):
                    act.wait_ge(max_done, TT * s + r + 1)
                    cols = score_cols(i)
                    nc.scalar.activation(probs[:, cols], probs[:, cols], ACT.Exp, bias=neg_max[:, r:r + 1],
                                         scale=-1.0, accum_out=row_sum[:, r:r + 1]).then_inc(exp_done, 1)

            def split_probs(s):
                for bank, width in enumerate(BANK_WIDTH):
                    act.wait_ge(pt_done, 3 * s + bank + 1)
                    cols = slice(BANK_START[bank], BANK_START[bank] + width)
                    nc.scalar.activation(probs_t[:, HI, cols], p_sc[bank][:, 0:width], ACT.Copy).then_inc(pt_hi, 1)

            def split_v(n, q, t, edge=False):
                act.wait_ge(v_done, TT * n + t + 1)
                bank = p_y if edge and t % 2 == 0 else p_v
                nc.scalar.activation(v[:, q, HI, t], bank[:], ACT.Copy).then_inc(v_hi, 1)

            def split_y(q, h, s):
                act.wait_ge(y_done, s + 1)
                nc.scalar.activation(y[:, q, HI, h], p_y[:], ACT.Copy).then_inc(y_hi, 1)

            def row(g, n, q, first=False, last=False):
                for h in range(HG):
                    s = HG * n + h
                    exps(s)
                    swap_halves(0, s + 1)
                    swap_halves(1, s + 1)
                    split_qk(0, s + 1)
                    split_probs(s)
                    if last:
                        for u in LOAD_AT[h][:2]:
                            split_next_w(g, u)
                    split_qk(1, s + 1)
                    if not last:
                        split_v(n + 1, 1 - q, h)
                    split_y(q, h, s)
                    if first:
                        split_w(g, O_UNIT + h, o_done, HG * B * g + ONE)
                    if last:
                        for u in LOAD_AT[h][2:]:
                            split_next_w(g, u)

            def split_next_w(g, u):
                what, h = kind(u)
                if what == "v":
                    split_w(g + 1, u, v_done, TT * B * (g + 1))
                else:
                    split_w(g + 1, u, qk_done[1], HG * B * g + (HG * (B - 1) + h + 1))

            for u in range(O_UNIT):
                split_first_w(u)
                if u == V_UNIT + KD - 1:
                    swap_halves(0, 0)
                    swap_halves(1, 0)
                    split_qk(0, 0)
                    split_qk(1, 0)
            with act.Fori(0, G) as g:
                for t in range(TT):
                    split_v(B * g, 0, t, edge=True)
                row(g, B * g, 0, first=True)
                with act.Fori(0, (B - 2) // 2) as i:
                    row(g, B * g + 2 * i + 1, 1)
                    row(g, B * g + 2 * i + 2, 0)
                row(g, B * g + (B - 1), 1, last=True)

        @block.gpsimd
        def _(pool):
            def split_w(g, u, first=False):
                pool.wait_ge(w_hi, UNITS * g + u + 1)
                stage = first_stage[u % STAGES] if first else w_stage[:, u % 2]
                nc.gpsimd.tensor_tensor(w_part(u, LO), stage, w_part(u, HI).bitcast(F32),
                                        ALU.subtract).then_inc(w_lo, 1)

            def normalise(s):
                for r, i in enumerate(ORDER):
                    if r % 2 == 0:
                        wait_alone(pool, inv_done, 2 * s + r // 2 + 1, pool_passed)
                    cols = score_cols(i)
                    nc.gpsimd.tensor_scalar(probs[:, cols], probs[:, cols], inv_sum[:, r:r + 1], 1.0,
                                            ALU.mult, ALU.mult).then_inc(prob_done, 1)

            def times_sin(c, s):
                pool.wait_ge(qk_swap[c], s + 1)
                nc.gpsimd.tensor_tensor(swap[:, c], swap[:, c], sin[:], ALU.mult).then_inc(qk_sin[c], 1)

            def row(g, n, q, first=False, last=False):
                for h in range(HG):
                    s = HG * n + h
                    normalise(s)
                    times_sin(0, s + 1)
                    times_sin(1, s + 1)
                    if first:
                        split_w(g, O_UNIT + h)
                    if last:
                        for u in LOAD_AT[h]:
                            split_w(g + 1, u)

            for u in range(O_UNIT):
                split_w(0, u, first=True)
                if u == V_UNIT + KD - 1:
                    pool.wait_ge(const_in, 64)
                    times_sin(0, 0)
                    times_sin(1, 0)
            with pool.Fori(0, G) as g:
                row(g, B * g, 0, first=True)
                with pool.Fori(0, (B - 2) // 2) as i:
                    row(g, B * g + 2 * i + 1, 1)
                    row(g, B * g + 2 * i + 2, 0)
                row(g, B * g + (B - 1), 1, last=True)

        @block.vector
        def _(dve):
            def masked_max(s):
                for bank, tiles in enumerate(SCORE_ORDER):
                    wait_alone(dve, score_done, 3 * s + bank + 1, dve_passed)
                    for i in tiles:
                        _, at, width = SCORE_AT[i]
                        r = ORDER.index(i)
                        nc.vector.tensor_tensor_reduce(
                            out=probs[:, score_cols(i)], in0=p_sc[bank][:, at:at + width],
                            in1=mask[:, T - width:], scale=-SCALE, scalar=3.0e38, op0=ALU.add, op1=ALU.min,
                            accum_out=neg_max[:, r:r + 1]).then_inc(max_done, 1)

            def invert(s):
                for r in range(2):
                    dve.wait_ge(exp_done, TT * s + 2 * r + 2)
                    nc.vector.reciprocal(inv_sum[:, 2 * r:2 * r + 2],
                                         row_sum[:, 2 * r:2 * r + 2]).then_inc(inv_done, 1)

            def times_cos(c, s):
                dve.wait_ge(qk_swap[c], s + 1)
                nc.vector.tensor_tensor(p_qk[c][0:2 * ROT, :], p_qk[c][0:2 * ROT, :], cos[:],
                                        ALU.mult).then_inc(qk_cos[c], 1)

            def rope(c, s):
                dve.wait_ge(qk_cos[c], s + 1)
                dve.wait_ge(qk_sin[c], s + 1)
                nc.vector.tensor_tensor(p_qk[c][0:2 * ROT, :], p_qk[c][0:2 * ROT, :], swap[:, c],
                                        ALU.add).then_inc(qk_rope[c], 1)

            def rest(to, bank, hi, signal):
                nc.vector.tensor_tensor(to, bank, hi.bitcast(F32), ALU.subtract).then_inc(signal, 1)

            def split_qk(c, s):
                dve.wait_ge(qk_hi[c], s + 1)
                rest(qk[:, c, LO], p_qk[c][:], qk[:, c, HI], qk_lo[c])

            def split_probs(s, rope_at):
                for bank, width in enumerate(BANK_WIDTH):
                    if bank == rope_at:
                        rope(1, s + 1)
                    dve.wait_ge(pt_hi, 3 * s + bank + 1)
                    cols = slice(BANK_START[bank], BANK_START[bank] + width)
                    rest(probs_t[:, LO, cols], p_sc[bank][:, 0:width], probs_t[:, HI, cols], pt_lo)

            def split_v(n, q, t, edge=False):
                dve.wait_ge(v_hi, TT * n + t + 1)
                bank = p_y if edge and t % 2 == 0 else p_v
                rest(v[:, q, LO, t], bank[:], v[:, q, HI, t], v_lo)

            def split_y(q, h, s):
                dve.wait_ge(y_hi, s + 1)
                rest(y[:, q, LO, h], p_y[:], y[:, q, HI, h], y_lo)

            def add_out(n, t, edge=False):
                bank = p_v if edge and t % 2 == 0 else p_o
                dve.wait_ge(acc_in[t], 16 * n + 16)
                dve.wait_ge(o_done, TT * n + t + 1 + ONE)
                nc.vector.scalar_tensor_tensor(acc[:, t], bank[:], 1.0 / 3.0, acc[:, t],
                                               ALU.mult, ALU.add).then_inc(acc_done, 1)

            def row(g, n, q, first=False, last=False):
                for h in range(HG):
                    s = HG * n + h
                    masked_max(s)
                    invert(s)
                    times_cos(0, s + 1)
                    rope(0, s + 1)
                    times_cos(1, s + 1)
                    split_qk(0, s + 1)
                    split_probs(s, 1 if first else None)
                    if not first:
                        rope(1, s + 1)
                    split_qk(1, s + 1)
                    if not last:
                        split_v(n + 1, 1 - q, h)
                    else:
                        add_out(n - 1, h)
                    split_y(q, h, s)
                    if not first and not last:
                        add_out(n - 1, h)

            for counted in (v_lo, y_lo, acc_done):
                dve.sem_inc(counted, ONE)
            dve.wait_ge(const_in, 64)
            for c in range(2):
                times_cos(c, 0)
                rope(c, 0)
                split_qk(c, 0)
            with dve.Fori(0, G) as g:
                for t in range(TT):
                    split_v(B * g, 0, t, edge=True)
                row(g, B * g, 0, first=True)
                with dve.Fori(0, (B - 2) // 2) as i:
                    row(g, B * g + 2 * i + 1, 1)
                    row(g, B * g + 2 * i + 2, 0)
                row(g, B * g + (B - 1), 1, last=True)
                for t in range(TT):
                    add_out(B * g + (B - 1), t, edge=True)


def build(nc, x, ffnw, ffns, down_s, wqk, wv, wo, const, out):
    xt_dram = nc.dram_tensor("xt_split", (B, P, 2, KD, T), F32, kind="Internal").ap()
    x_tiles = x.rearrange("b (t p) d -> b p t d", p=P)
    out_tiles = out.rearrange("b (t p) d -> b p t d", p=P)
    with (
        nc.sbuf_tensor("xt", [P, 2, 2, KD, T], F32R) as xt,
        nc.sbuf_tensor("w_stage", [P, 2, 512], F32) as w_stage,
        nc.semaphore("first_in0") as first_in0,
        nc.semaphore("first_in1") as first_in1,
        nc.semaphore("x_in0") as x_in0,
        nc.semaphore("x_in1") as x_in1,
    ):
        ffn_phase(nc, xt, x_in0, w_stage, [first_in0, first_in1], wqk, x_tiles, ffnw, ffns, down_s, const, xt_dram, out_tiles)
        attention_phase(nc, xt, [x_in0, x_in1], w_stage, [first_in0, first_in1], wqk, wv, wo, const, xt_dram, out_tiles)


def constants(np):
    table = np.zeros((P, 3 * T + P), np.float32)
    table[:, C_MASK + T - P:C_MASK + T] = np.triu(np.full((P, P), -1e30, np.float32), 1)
    table[:, C_IDENT:C_IDENT + P] = np.eye(P, dtype=np.float32)
    freq = np.float32(1.0 / 1024.0) ** np.linspace(0.0, 1.0, ROT, dtype=np.float32)
    angle = freq[:, None] * np.arange(T, dtype=np.float32)[None, :]
    table[0:ROT, C_COS:C_COS + T] = table[ROT:2 * ROT, C_COS:C_COS + T] = np.cos(angle)
    table[0:ROT, C_SIN:C_SIN + T] = np.sin(angle)
    table[ROT:2 * ROT, C_SIN:C_SIN + T] = -np.sin(angle)
    return table


def kernel(L0_attn_x, L0_attn_Wq, L0_attn_Wk, L0_attn_Wv, L0_attn_Wo, L0_ffn_gate_w, L0_ffn_up_w,
           L0_ffn_down_w, L0_ffn_gate_s, L0_ffn_up_s, L0_ffn_down_s):
    import numpy as np
    import concourse.bacc as bacc
    from concourse.bass_utils import run_bass_kernel_spmd

    def tiles(w):
        return np.asarray(w).T.reshape(KD, P, -1).transpose(1, 0, 2)

    order = np.r_[0:ROT, DH // 2:DH // 2 + ROT, ROT:DH // 2, DH // 2 + ROT:DH]
    wqk = np.stack([tiles(w).reshape(P, KD, G, HG, DH)[..., order].transpose(2, 3, 0, 1, 4)
                    for w in (L0_attn_Wq, L0_attn_Wk)], axis=2)
    wv = tiles(L0_attn_Wv).reshape(P, KD, G, HG * DH).transpose(2, 1, 0, 3)
    wo = np.asarray(L0_attn_Wo).T.reshape(G, HG, P, D)
    gate_up = [tiles(w).reshape(P, KD, J, P).transpose(2, 0, 1, 3).reshape(J, P, KD * P)
               for w in (L0_ffn_gate_w, L0_ffn_up_w)]
    ffnw = np.stack([*gate_up, np.asarray(L0_ffn_down_w).T.reshape(J, P, D)], axis=1)
    arrays = {
        "x": np.asarray(L0_attn_x),
        "ffnw": ffnw.reshape(3 * J, P, 512),
        "ffns": np.stack([np.asarray(s).reshape(J, P).T for s in (L0_ffn_gate_s, L0_ffn_up_s)], axis=1),
        "down_s": np.broadcast_to(np.asarray(L0_ffn_down_s), (P, D)),
        "wqk": wqk.reshape(G, 2 * HG, P, KD * DH),
        "wv": wv,
        "wo": wo,
        "const": constants(np),
    }
    arrays = {f"in_{name}": np.ascontiguousarray(a) for name, a in arrays.items()}
    nc = bacc.Bacc("TRN2", target_bir_lowering=False, num_devices=1)
    args = [nc.dram_tensor(name, a.shape, mybir.dt.from_np(a.dtype), kind="ExternalInput").ap()
            for name, a in arrays.items()]
    out = nc.dram_tensor("out", (B, T, D), F32, kind="ExternalOutput").ap()
    build(nc, *args, out)
    return run_bass_kernel_spmd(nc, [arrays], core_ids=[0]).results[0]["out"]
```
